# Optimizing a Trainium2 kernel written in Bass

```python
import numpy as np
import jax
import jax.numpy as jnp

def _softmax(x, axis=-1):
    return jax.nn.softmax(x, axis=axis)

def _gelu(x):
    return jax.nn.gelu(x, approximate=True)

def _silu(x):
    return jax.nn.silu(x)

def _sigmoid(x):
    return jax.nn.sigmoid(x)

def _layernorm(x, axis=-1, eps=1e-05):
    m = jnp.mean(x, axis=axis, keepdims=True)
    v = jnp.var(x, axis=axis, keepdims=True)
    return (x - m) / jnp.sqrt(v + eps)

def _scatter_add(tgt, idx, src, axis=0):
    return tgt.at[idx].add(src)

def _segment_sum(src, seg, n):
    return jax.ops.segment_sum(src, seg, n)
kernel_name = 'mk_adj_preln_d1_adj_r2_455312'

def setup_inputs(seed: int=0):
    np.random.seed(seed)
    _w = jnp.asarray

    def _rec_inputs():
        import jax
        import jax.numpy as jnp
        _gk = jax.random.key(seed)
        x = -0.0005207 + 1.001 * jax.random.normal(jax.random.fold_in(_gk, 1), (8192, 128), jnp.float32)
        _a = jax.random.bernoulli(jax.random.fold_in(_gk, 2), 0.000976562, (8192, 8192))
        _a = jnp.logical_or(_a, jnp.eye(8192, dtype=bool))
        _af = _a.astype(jnp.float32)
        _af = _af * jax.random.uniform(jax.random.fold_in(_gk, 3), (8192, 8192), jnp.float32, 0.05, 1)
        adj = _af
        return (x, adj)
    x, adj = _rec_inputs()

    def _L0_gnn_setup():
        import jax, jax.numpy as jnp
        import numpy as np
        ALPHA = 0.1
        N, F = (8192, 128)
        key = jax.random.key(seed)
        k1, k2, k3 = jax.random.split(key, 3)
        x = jax.random.normal(k1, (N, F), dtype=jnp.float32)
        adj = jax.random.uniform(k2, (N, N), dtype=jnp.float32)
        h = jax.random.normal(k3, (N, F), dtype=jnp.float32)
        return {'x': x, 'adj': adj, 'h': h}
    _L0_gnn_all = _L0_gnn_setup()
    _L0_gnn_in = {k: v for k, v in _L0_gnn_all.items() if k in ('h',)}
    del _L0_gnn_all
    return {'x': x, 'adj': adj, 'L0_gnn_h': _L0_gnn_in['h']}

def reference(x, adj, L0_gnn_h):
    import jax
    import jax.numpy as jnp

    def _L0_gnn_ref(x, adj, h):
        import jax, jax.numpy as jnp
        import numpy as np
        ALPHA = 0.1
        N, F = (8192, 128)
        return (1.0 - ALPHA) * (adj @ x) + ALPHA * h
    h = jnp.maximum(_layernorm(x, axis=-1), 0.0)
    x = x + _L0_gnn_ref(h, adj, L0_gnn_h)
    return x

_drawn_inputs = setup_inputs


def setup_inputs(seed=0):
    import zlib

    import numpy as np

    out = dict(_drawn_inputs(seed))
    spreads = {}
    factors = {}
    for name, (base, spread) in spreads.items():
        noise = np.random.default_rng([zlib.crc32(name.encode()), seed]).standard_normal(out[name].shape)
        drawn = base * np.exp(spread * noise) if base else spread * noise
        out[name] = jnp.asarray(drawn.astype(out[name].dtype))
    for name, factor in factors.items():
        out[name] = (out[name] * factor).astype(out[name].dtype)
    return out
```

```python
import concourse.bass as bass
from concourse import mybir
from contextlib import ExitStack


def gnn_layer_kernel(nc: bass.Bass, x: bass.AP, adj: bass.AP, L0_gnn_h: bass.AP, out: bass.AP):
    fp32 = mybir.dt.float32
    ALU = mybir.AluOpType
    ACT = mybir.ActivationFunctionType

    ALPHA, EPS = 0.1, 1e-5
    P, QUAD = 128, 32
    N, F = x.shape
    NQ = P // QUAD
    KQ = N // NQ
    CHUNK = 512
    CHUNKS = N // CHUNK
    BLOCKS = CHUNK // QUAD
    W = 512
    WINDOWS = KQ // W
    TILES = W // QUAD
    PAIRS = TILES // 2
    CPAIRS = WINDOWS * PAIRS
    TRING = 4
    PIECES = 4
    PW = W // PIECES
    S = CHUNK // P
    LOADED = 16 * NQ

    adj_v = adj.rearrange("(u j r) (q w c) -> u q w r j c", j=BLOCKS, r=QUAD, q=NQ, w=WINDOWS)
    x_k = x.rearrange("(q w t c) f -> q w c t f", q=NQ, w=WINDOWS, c=QUAD)
    x_m = x.rearrange("(u p s) f -> u p s f", p=P, s=S)
    h_m = L0_gnn_h.rearrange("(u p s) f -> u p s f", p=P, s=S)
    out_m = out.rearrange("(u p s) f -> u p s f", p=P, s=S)

    ctx = ExitStack()
    with ctx:
        def sb(name, shape):
            return ctx.enter_context(nc.sbuf_tensor(name, shape, fp32))

        def sem(name):
            return ctx.enter_context(nc.semaphore(name))

        adj_sb = sb("adj_sb", [P, WINDOWS, BLOCKS, W])
        adj_t = sb("adj_t", [P, TRING, 2, CHUNK])
        h_sb = sb("h_sb", [P, WINDOWS, TILES, F])
        acc_sb = sb("acc_sb", [P, CHUNK])
        x_res = sb("x_res", [P, S, F])
        h_res = sb("h_res", [P, S, F])
        out_sb = sb("out_sb", [P, S, F])
        ident = sb("ident", [P, P])
        stats = sb("stats", [P, TILES, 6])
        moments = sb("moments", [P, WINDOWS, TILES, 2])
        var_eps = sb("var_eps", [P, TILES])
        root = sb("root", [P, WINDOWS, TILES])
        recip = sb("recip", [P, TILES])
        newton = sb("newton", [P, TILES])
        rstd = sb("rstd", [P, WINDOWS, TILES])
        shift = sb("shift", [P, WINDOWS, TILES])

        acc = ctx.enter_context(nc.psum_tensor("acc", [P, 2, CHUNK], fp32))
        back = ctx.enter_context(nc.psum_tensor("back", [P, S, F], fp32))

        piece_loaded = [sem(f"piece_loaded{b}") for b in range(PIECES)]
        window_loaded = [sem(f"window_loaded{w}") for w in range(WINDOWS)]
        x_loaded = [sem(f"x_loaded{w}") for w in range(WINDOWS)]
        ident_zeroed = sem("ident_zeroed")
        ident_ready = sem("ident_ready")
        stat_step = sem("stat_step")
        var_ready = sem("var_ready")
        root_ready = sem("root_ready")
        scales_ready = sem("scales_ready")
        h_ready = sem("h_ready")
        pair_transposed = sem("pair_transposed")
        pair_used = sem("pair_used")
        acc_copied = sem("acc_copied")
        turned_back = sem("turned_back")
        res_loaded = sem("res_loaded")
        res_summed = sem("res_summed")
        out_ready = sem("out_ready")
        out_stored = sem("out_stored")

        block = ctx.enter_context(nc.Block())

        @block.gpsimd
        def _(pool):
            nc.gpsimd.memset(ident[:, :], 0.0).then_inc(ident_zeroed, 1)
            pool.wait_ge(ident_zeroed, 1)
            nc.gpsimd.affine_select(out=ident[:, :], in_=ident[:, :], compare_op=ALU.not_equal, fill=1.0,
                                    base=0, pattern=[[-1, P]], channel_multiplier=1).then_inc(ident_ready, 1)

        @block.sync
        def _(sp):
            def load_window(u, w):
                for q in range(NQ):
                    sp.dma_start(adj_sb[q * QUAD:(q + 1) * QUAD, w, :, :],
                                 adj_v[u, q, w]).then_inc(window_loaded[w], 16)

            for b in range(PIECES):
                for q in range(NQ):
                    sp.dma_start(adj_sb[q * QUAD:(q + 1) * QUAD, 0, :, b * PW:(b + 1) * PW],
                                 adj_v[0, q, 0, :, :, b * PW:(b + 1) * PW]).then_inc(piece_loaded[b], 16)
            for w in range(1, WINDOWS):
                load_window(0, w)
            with sp.Fori(1, CHUNKS) as u:
                for w in range(WINDOWS):
                    sp.wait_ge(pair_transposed, (u - 1) * CPAIRS + (w + 1) * PAIRS)
                    load_window(u, w)

        @block.scalar
        def _(act):
            for w in range(WINDOWS):
                for q in range(NQ):
                    act.dma_start(h_sb[q * QUAD:(q + 1) * QUAD, w, :, :], x_k[q, w]).then_inc(x_loaded[w], 16)

            for w in range(WINDOWS):
                act.wait_ge(var_ready, w + 1)
                nc.scalar.activation(root[:, w, :], var_eps[:, :], ACT.Sqrt).then_inc(root_ready, 1)
                act.wait_ge(scales_ready, w + 1)
                for t in range(TILES):
                    nc.scalar.activation(h_sb[:, w, t, :], h_sb[:, w, t, :], ACT.Relu,
                                         bias=shift[:, w, t:t + 1],
                                         scale=rstd[:, w, t:t + 1]).then_inc(h_ready, 1)

            def finish_chunk(u, parity, first):
                if not first:
                    act.wait_ge(out_ready, u)
                    act.wait_ge(out_stored, 16 * u)
                act.dma_start(x_res[:, :, :], x_m[u]).then_inc(res_loaded, 16)
                act.dma_start(h_res[:, :, :], h_m[u]).then_inc(res_loaded, 16)
                act.wait_ge(pair_used, (u + 1) * CPAIRS)
                if not first:
                    act.wait_ge(turned_back, u)
                nc.scalar.copy(acc_sb[:, :], acc[:, parity, :]).then_inc(acc_copied, 1)
                act.wait_ge(out_ready, u + 1)
                act.dma_start(out_m[u], out_sb[:, :, :]).then_inc(out_stored, 16)

            finish_chunk(0, 0, True)
            finish_chunk(1, 1, False)
            with act.Fori(1, CHUNKS // 2) as two:
                finish_chunk(2 * two, 0, False)
                finish_chunk(2 * two + 1, 1, False)
            act.wait_ge(out_stored, 16 * CHUNKS)

        @block.vector
        def _(dve):
            steps = [0]

            def step(ins):
                steps[0] += 1
                ins.then_inc(stat_step, 1)
                dve.wait_ge(stat_step, steps[0])

            def layernorm_scales(w):
                dve.wait_ge(x_loaded[w], LOADED)
                for t in range(TILES):
                    last = nc.vector.bn_stats(stats[:, t, :], h_sb[:, w, t, :])
                step(last)
                for t in range(TILES):
                    last = nc.vector.bn_aggr(moments[:, w, t, :], stats[:, t, :])
                step(last)
                if w > 0:
                    dve.wait_ge(root_ready, w)
                nc.vector.tensor_scalar(var_eps[:, :], moments[:, w, :, 1], EPS, None,
                                        ALU.add).then_inc(var_ready, 1)
                dve.wait_ge(root_ready, w + 1)
                step(nc.vector.reciprocal(recip[:, :], root[:, w, :]))
                step(nc.vector.tensor_tensor(newton[:, :], var_eps[:, :], recip[:, :], ALU.mult))
                step(nc.vector.tensor_tensor(newton[:, :], newton[:, :], root[:, w, :], ALU.add))
                step(nc.vector.tensor_scalar(newton[:, :], newton[:, :], 0.5, None, ALU.mult))
                step(nc.vector.reciprocal(rstd[:, w, :], newton[:, :]))
                nc.vector.scalar_tensor_tensor(out=shift[:, w, :], in0=moments[:, w, :, 0], scalar=-1.0,
                                               in1=rstd[:, w, :], op0=ALU.mult,
                                               op1=ALU.mult).then_inc(scales_ready, 1)

            def transpose_pair(u, w, g, free):
                if free:
                    dve.wait_ge(pair_used, u * CPAIRS + w * PAIRS + g + 1 - TRING)
                blocks = adj_sb[:, w, :, 2 * g * QUAD:2 * (g + 1) * QUAD]
                nc.vector.transpose(adj_t[:, g % TRING, :, :].rearrange("p t (j r) -> p t j r", r=QUAD),
                                    blocks.rearrange("p j (t c) -> p t j c", c=QUAD)).then_inc(pair_transposed, 1)

            def write_out(u):
                dve.wait_ge(res_loaded, 32 * (u + 1))
                nc.vector.scalar_tensor_tensor(out=x_res[:, :, :], in0=h_res[:, :, :], scalar=ALPHA,
                                               in1=x_res[:, :, :], op0=ALU.mult, op1=ALU.add).then_inc(res_summed, 1)
                dve.wait_ge(res_summed, u + 1)
                dve.wait_ge(turned_back, u + 1)
                nc.vector.scalar_tensor_tensor(out=out_sb[:, :, :], in0=back[:, :, :], scalar=1.0 - ALPHA,
                                               in1=x_res[:, :, :], op0=ALU.mult, op1=ALU.add).then_inc(out_ready, 1)

            def transpose_chunk(u):
                for w in range(WINDOWS):
                    dve.wait_ge(window_loaded[w], u * LOADED if w == 0 else (u + 1) * LOADED)
                    for g in range(PAIRS):
                        transpose_pair(u, w, g, True)
                    if w == 1:
                        write_out(u - 1)

            for w in range(WINDOWS):
                layernorm_scales(w)
                if w > 0:
                    dve.wait_ge(window_loaded[w], LOADED)
                for g in range(PAIRS):
                    if w == 0 and g % (PAIRS // PIECES) == 0:
                        dve.wait_ge(piece_loaded[g // (PAIRS // PIECES)], LOADED)
                    transpose_pair(0, w, g, w > 0 or g >= TRING)
            with dve.Fori(1, CHUNKS) as u:
                transpose_chunk(u)
            write_out(CHUNKS - 1)

        @block.tensor
        def _(pe):
            def multiply_window(u, w, parity, first):
                for g in range(PAIRS):
                    pe.wait_ge(pair_transposed, u * CPAIRS + w * PAIRS + g + 1)
                    for i in range(2):
                        t = 2 * g + i
                        if first:
                            pe.wait_ge(h_ready, w * TILES + t + 1)
                        last = nc.tensor.matmul(acc[:, parity, :], h_sb[:, w, t, :], adj_t[:, g % TRING, i, :],
                                                start=(w == 0 and t == 0),
                                                stop=(w == WINDOWS - 1 and t == TILES - 1))
                    last.then_inc(pair_used, 1)

            def turn_back(u, first):
                pe.wait_ge(acc_copied, u + 1)
                if not first:
                    pe.wait_ge(out_ready, u)
                columns = acc_sb[:, :].rearrange("f (p s) -> f s p", s=S)
                for s in range(S):
                    last = nc.tensor.transpose(back[:, s, :], columns[:, s, :], ident[:, :])
                last.then_inc(turned_back, 1)

            def multiply_chunk(u, parity, first, second):
                if not (first or second):
                    pe.wait_ge(acc_copied, u - 1)
                multiply_window(u, 0, parity, first)
                if not first:
                    turn_back(u - 1, second)
                for w in range(1, WINDOWS):
                    multiply_window(u, w, parity, first)

            multiply_chunk(0, 0, True, False)
            pe.wait_ge(ident_ready, 1)
            multiply_chunk(1, 1, False, True)
            with pe.Fori(1, CHUNKS // 2) as two:
                multiply_chunk(2 * two, 0, False, False)
                multiply_chunk(2 * two + 1, 1, False, False)
            turn_back(CHUNKS - 1, False)


_INS = ['x', 'adj', 'L0_gnn_h']
_OUTS = [((8192, 128), 'float32')]


def kernel(**inputs):
    import numpy as _np
    import concourse.bacc as _bacc
    from concourse import mybir as _mybir
    from concourse.bass_utils import run_bass_kernel_spmd as _run

    nc = _bacc.Bacc("TRN2", target_bir_lowering=False, num_devices=1)
    arrays, args = {}, []
    for name in _INS:
        a = _np.ascontiguousarray(inputs[name])
        arrays[f"in_{name}_dram"] = a
        args.append(nc.dram_tensor(f"in_{name}_dram", a.shape, _mybir.dt.from_np(a.dtype), kind="ExternalInput").ap())
    for i, (shape, dtype) in enumerate(_OUTS):
        dt = _mybir.dt.from_np(_np.dtype(dtype))
        args.append(nc.dram_tensor(f"out_{i}_dram", shape, dt, kind="ExternalOutput").ap())
    gnn_layer_kernel(nc, *args)
    r = _run(nc, [arrays], core_ids=[0])
    got = tuple(r.results[0][f"out_{i}_dram"] for i in range(len(_OUTS)))
    return got[0]
```

```python
import concourse.bass as bass
from concourse import mybir
from contextlib import ExitStack


def gnn_layer_kernel(nc: bass.Bass, x: bass.AP, adj: bass.AP, L0_gnn_h: bass.AP, out: bass.AP):
    fp32 = mybir.dt.float32
    fp32r = mybir.dt.float32r
    ALU = mybir.AluOpType
    ACT = mybir.ActivationFunctionType

    ALPHA, EPS = 0.1, 1e-5
    P, QUAD = 128, 32
    N, F = x.shape
    NQ = P // QUAD
    KQ = N // NQ
    CHUNK = 512
    CHUNKS = N // CHUNK
    BLOCKS = CHUNK // QUAD
    W = 256
    WINDOWS = KQ // W
    TILES = W // QUAD
    PAIRS = TILES // 2
    CPAIRS = WINDOWS * PAIRS
    ADJ_RING = 4
    AHEAD = ADJ_RING - 1
    RING = 4
    PIECES = 2
    PW = W // PIECES
    S = CHUNK // P
    LOADED = 16 * NQ

    COPY_AT = 2
    WRITE_AT = 5

    SPLIT = [(w, g) for w in range(WINDOWS) for g in range(PAIRS) if g % 2 == 1]
    PLAIN = [(w, g) for w in range(WINDOWS) for g in range(PAIRS) if (w, g) not in SPLIT]
    assert len(SPLIT) % RING == 0 and len(PLAIN) % RING == 0

    def pair(u, w, g):
        return u * CPAIRS + w * PAIRS + g

    def slot(kind, w, g):
        return kind.index((w, g)) % RING

    def held_slot_before(kind, u, w, g):
        i = kind.index((w, g)) - RING
        return pair(u, *kind[i]) if i >= 0 else pair(u - 1, *kind[i])

    adj_v = adj.rearrange("(u j r) (q w c) -> u q w r j c", j=BLOCKS, r=QUAD, q=NQ, w=WINDOWS)
    x_k = x.rearrange("(q w t c) f -> q w c t f", q=NQ, w=WINDOWS, c=QUAD)
    x_m = x.rearrange("(u p s) f -> u p s f", p=P, s=S)
    h_m = L0_gnn_h.rearrange("(u p s) f -> u p s f", p=P, s=S)
    out_m = out.rearrange("(u p s) f -> u p s f", p=P, s=S)

    ctx = ExitStack()
    with ctx:
        def sb(name, shape, dt=fp32):
            return ctx.enter_context(nc.sbuf_tensor(name, shape, dt))

        def sem(name):
            return ctx.enter_context(nc.semaphore(name))

        adj_sb = sb("adj_sb", [P, ADJ_RING, BLOCKS, W])
        plain_t = sb("plain_t", [P, RING, 2, CHUNK])
        raw_t = sb("raw_t", [P, RING, 2, CHUNK])
        a_hi = sb("a_hi", [P, RING, 2, CHUNK], fp32r)
        a_lo = sb("a_lo", [P, RING, 2, CHUNK], fp32r)
        h_sb = sb("h_sb", [P, WINDOWS, TILES, F])
        h_hi = sb("h_hi", [P, len(SPLIT), 2, F], fp32r)
        h_lo = sb("h_lo", [P, len(SPLIT), 2, F], fp32r)
        acc_sb = sb("acc_sb", [P, CHUNK])
        x_res = sb("x_res", [P, S, F])
        h_res = sb("h_res", [P, S, F])
        out_sb = sb("out_sb", [P, S, F])
        ident = sb("ident", [P, P])
        stats = sb("stats", [P, TILES, 6])
        moments = sb("moments", [P, WINDOWS, TILES, 2])
        var_eps = sb("var_eps", [P, TILES])
        root = sb("root", [P, WINDOWS, TILES])
        recip = sb("recip", [P, TILES])
        newton = sb("newton", [P, TILES])
        rstd = sb("rstd", [P, WINDOWS, TILES])
        shift = sb("shift", [P, WINDOWS, TILES])

        acc = ctx.enter_context(nc.psum_tensor("acc", [P, 2, CHUNK], fp32))
        back = ctx.enter_context(nc.psum_tensor("back", [P, S, F], fp32))

        piece_loaded = [sem(f"piece_loaded{b}") for b in range(PIECES)]
        window_loaded = [sem(f"window_loaded{w}") for w in range(ADJ_RING)]
        x_loaded = [sem(f"x_loaded{w}") for w in range(WINDOWS)]
        ident_zeroed = sem("ident_zeroed")
        ident_ready = sem("ident_ready")
        stat_step = sem("stat_step")
        var_ready = sem("var_ready")
        root_ready = sem("root_ready")
        scales_ready = sem("scales_ready")
        h_ready = sem("h_ready")
        h_hi_ready = sem("h_hi_ready")
        h_lo_ready = sem("h_lo_ready")
        pair_transposed = sem("pair_transposed")
        a_hi_ready = sem("a_hi_ready")
        a_lo_ready = sem("a_lo_ready")
        pair_used = sem("pair_used")
        acc_copied = sem("acc_copied")
        turned_back = sem("turned_back")
        res_loaded = sem("res_loaded")
        res_summed = sem("res_summed")
        out_ready = sem("out_ready")
        out_stored = sem("out_stored")

        block = ctx.enter_context(nc.Block())

        def load_window(eng, quadrants, u, w):
            for q in quadrants:
                eng.dma_start(adj_sb[q * QUAD:(q + 1) * QUAD, w % ADJ_RING, :, :],
                              adj_v[u, q, w]).then_inc(window_loaded[w % ADJ_RING], 16)

        def load_first_window(eng, quadrants):
            for b in range(PIECES):
                for q in quadrants:
                    eng.dma_start(adj_sb[q * QUAD:(q + 1) * QUAD, 0, :, b * PW:(b + 1) * PW],
                                  adj_v[0, q, 0, :, :, b * PW:(b + 1) * PW]).then_inc(piece_loaded[b], 16)

        def load_x_window(eng, quadrants, w):
            for q in quadrants:
                eng.dma_start(h_sb[q * QUAD:(q + 1) * QUAD, w, :, :], x_k[q, w]).then_inc(x_loaded[w], 16)

        def load_first_windows(eng, quadrants):
            load_x_window(eng, quadrants, 0)
            load_first_window(eng, quadrants)
            for w in range(1, ADJ_RING):
                load_x_window(eng, quadrants, w)
                load_window(eng, quadrants, 0, w)
            for w in range(ADJ_RING, WINDOWS):
                load_x_window(eng, quadrants, w)

        @block.gpsimd
        def _(pool):
            nc.gpsimd.memset(ident[:, :], 0.0).then_inc(ident_zeroed, 1)
            pool.wait_ge(ident_zeroed, 1)
            nc.gpsimd.affine_select(out=ident[:, :], in_=ident[:, :], compare_op=ALU.not_equal, fill=1.0,
                                    base=0, pattern=[[-1, P]], channel_multiplier=1).then_inc(ident_ready, 1)

            def low_part(u, i):
                pool.wait_ge(a_hi_ready, u * len(SPLIT) + i + 1)
                nc.gpsimd.tensor_tensor(a_lo[:, i % RING, :, :], raw_t[:, i % RING, :, :],
                                        a_hi[:, i % RING, :, :].bitcast(fp32), ALU.subtract).then_inc(a_lo_ready, 1)

            for i, (w, g) in enumerate(SPLIT):
                pool.wait_ge(h_hi_ready, i + 1)
                nc.gpsimd.tensor_tensor(h_lo[:, i, :, :], h_sb[:, w, 2 * g:2 * g + 2, :],
                                        h_hi[:, i, :, :].bitcast(fp32), ALU.subtract).then_inc(h_lo_ready, 1)
                low_part(0, i)
            with pool.Fori(1, CHUNKS) as u:
                for i in range(len(SPLIT)):
                    low_part(u, i)

        @block.sync
        def _(sp):
            load_first_windows(sp, (0, 1))
            for w in range(ADJ_RING, WINDOWS):
                sp.wait_ge(pair_transposed, pair(0, w - ADJ_RING + 1, 0))
                load_window(sp, (0, 1), 0, w)
            with sp.Fori(1, CHUNKS) as u:
                for w in range(WINDOWS):
                    sp.wait_ge(pair_transposed, pair(u, w - ADJ_RING + 1, 0))
                    load_window(sp, (0, 1), u, w)

        @block.scalar
        def _(act):
            load_first_windows(act, (2, 3))

            def load_ahead(u, w, first, last):
                if first and w == 0 or last and w + AHEAD >= WINDOWS:
                    return
                act.wait_ge(pair_transposed, pair(u, w, 0))
                if w + AHEAD < WINDOWS:
                    load_window(act, (2, 3), u, w + AHEAD)
                else:
                    load_window(act, (2, 3), u + 1, w + AHEAD - WINDOWS)

            def layernorm_window(w):
                act.wait_ge(var_ready, w + 1)
                nc.scalar.activation(root[:, w, :], var_eps[:, :], ACT.Sqrt).then_inc(root_ready, 1)
                act.wait_ge(scales_ready, w + 1)
                for t in range(TILES):
                    nc.scalar.activation(h_sb[:, w, t, :], h_sb[:, w, t, :], ACT.Relu,
                                         bias=shift[:, w, t:t + 1],
                                         scale=rstd[:, w, t:t + 1]).then_inc(h_ready, 1)
                for g in range(PAIRS):
                    if (w, g) in SPLIT:
                        act.wait_ge(h_ready, w * TILES + 2 * g + 2)
                        nc.scalar.copy(h_hi[:, SPLIT.index((w, g)), :, :],
                                       h_sb[:, w, 2 * g:2 * g + 2, :]).then_inc(h_hi_ready, 1)

            def high_part(u, w, g, first):
                i = SPLIT.index((w, g))
                act.wait_ge(pair_transposed, pair(u, w, g) + 1)
                if not first or i >= RING:
                    act.wait_ge(pair_used, held_slot_before(SPLIT, u, w, g) + 1)
                nc.scalar.copy(a_hi[:, i % RING, :, :], raw_t[:, i % RING, :, :]).then_inc(a_hi_ready, 1)

            def load_residual(u, very_first):
                if not very_first:
                    act.wait_ge(out_ready, u)
                    act.wait_ge(out_stored, 16 * u)
                act.dma_start(x_res[:, :, :], x_m[u]).then_inc(res_loaded, 16)
                act.dma_start(h_res[:, :, :], h_m[u]).then_inc(res_loaded, 16)

            def copy_acc(u, parity, very_first):
                act.wait_ge(pair_used, pair(u + 1, 0, 0))
                if not very_first:
                    act.wait_ge(turned_back, u)
                nc.scalar.copy(acc_sb[:, :], acc[:, parity, :]).then_inc(acc_copied, 1)

            def store(u):
                act.wait_ge(out_ready, u + 1)
                act.dma_start(out_m[u], out_sb[:, :, :]).then_inc(out_stored, 16)

            def chunk(u, parity, first=False, second=False, last=False):
                for w in range(WINDOWS):
                    load_ahead(u, w, first, last)
                    if first:
                        layernorm_window(w)
                    elif w == 0:
                        load_residual(u - 1, second)
                    for g in range(PAIRS):
                        if (w, g) in SPLIT:
                            high_part(u, w, g, first)
                    if w == COPY_AT and not first:
                        copy_acc(u - 1, 1 - parity, second)
                if not first:
                    store(u - 1)

            chunk(0, 0, first=True)
            chunk(1, 1, second=True)
            with act.Fori(1, CHUNKS // 2 - 1) as two:
                chunk(2 * two, 0)
                chunk(2 * two + 1, 1)
            chunk(CHUNKS - 2, 0)
            chunk(CHUNKS - 1, 1, last=True)
            load_residual(CHUNKS - 1, False)
            copy_acc(CHUNKS - 1, 1, False)
            store(CHUNKS - 1)
            act.wait_ge(out_stored, 16 * CHUNKS)

        @block.vector
        def _(dve):
            steps = [0]

            def step(ins):
                steps[0] += 1
                ins.then_inc(stat_step, 1)
                dve.wait_ge(stat_step, steps[0])

            def layernorm_scales(w):
                dve.wait_ge(x_loaded[w], LOADED)
                for t in range(TILES):
                    last = nc.vector.bn_stats(stats[:, t, :], h_sb[:, w, t, :])
                step(last)
                for t in range(TILES):
                    last = nc.vector.bn_aggr(moments[:, w, t, :], stats[:, t, :])
                step(last)
                if w > 0:
                    dve.wait_ge(root_ready, w)
                nc.vector.tensor_scalar(var_eps[:, :], moments[:, w, :, 1], EPS, None,
                                        ALU.add).then_inc(var_ready, 1)
                dve.wait_ge(root_ready, w + 1)
                step(nc.vector.reciprocal(recip[:, :], root[:, w, :]))
                step(nc.vector.tensor_tensor(newton[:, :], var_eps[:, :], recip[:, :], ALU.mult))
                step(nc.vector.tensor_tensor(newton[:, :], newton[:, :], root[:, w, :], ALU.add))
                step(nc.vector.tensor_scalar(newton[:, :], newton[:, :], 0.5, None, ALU.mult))
                step(nc.vector.reciprocal(rstd[:, w, :], newton[:, :]))
                nc.vector.scalar_tensor_tensor(out=shift[:, w, :], in0=moments[:, w, :, 0], scalar=-1.0,
                                               in1=rstd[:, w, :], op0=ALU.mult,
                                               op1=ALU.mult).then_inc(scales_ready, 1)

            def transpose_pair(u, w, g, first):
                if (w, g) in SPLIT:
                    i = SPLIT.index((w, g))
                    to = raw_t[:, i % RING, :, :]
                    if not first or i >= RING:
                        dve.wait_ge(a_lo_ready, u * len(SPLIT) + i + 1 - RING)
                else:
                    i = PLAIN.index((w, g))
                    to = plain_t[:, i % RING, :, :]
                    if not first or i >= RING:
                        dve.wait_ge(pair_used, held_slot_before(PLAIN, u, w, g) + 1)
                blocks = adj_sb[:, w % ADJ_RING, :, 2 * g * QUAD:2 * (g + 1) * QUAD]
                nc.vector.transpose(to.rearrange("p t (j r) -> p t j r", r=QUAD),
                                    blocks.rearrange("p j (t c) -> p t j c", c=QUAD)).then_inc(pair_transposed, 1)

            def write_out(u):
                dve.wait_ge(res_loaded, 32 * (u + 1))
                nc.vector.scalar_tensor_tensor(out=x_res[:, :, :], in0=h_res[:, :, :], scalar=ALPHA,
                                               in1=x_res[:, :, :], op0=ALU.mult, op1=ALU.add).then_inc(res_summed, 1)
                dve.wait_ge(res_summed, u + 1)
                dve.wait_ge(turned_back, u + 1)
                nc.vector.scalar_tensor_tensor(out=out_sb[:, :, :], in0=back[:, :, :], scalar=1.0 - ALPHA,
                                               in1=x_res[:, :, :], op0=ALU.mult, op1=ALU.add).then_inc(out_ready, 1)

            def wait_for_window(u, w):
                loads = u * (WINDOWS // ADJ_RING) + w // ADJ_RING + (w % ADJ_RING > 0)
                dve.wait_ge(window_loaded[w % ADJ_RING], loads * LOADED)

            for w in range(WINDOWS):
                layernorm_scales(w)
                if w > 0:
                    wait_for_window(0, w)
                for g in range(PAIRS):
                    if w == 0 and g % (PAIRS // PIECES) == 0:
                        dve.wait_ge(piece_loaded[g // (PAIRS // PIECES)], LOADED)
                    transpose_pair(0, w, g, True)
            with dve.Fori(1, CHUNKS) as u:
                for w in range(WINDOWS):
                    wait_for_window(u, w)
                    for g in range(PAIRS):
                        transpose_pair(u, w, g, False)
                    if w == WRITE_AT:
                        write_out(u - 1)
            write_out(CHUNKS - 1)

        @block.tensor
        def _(pe):
            def multiply_plain(u, w, g, parity, first):
                pe.wait_ge(pair_transposed, pair(u, w, g) + 1)
                for i in range(2):
                    t = 2 * g + i
                    if first:
                        pe.wait_ge(h_ready, w * TILES + t + 1)
                    last = nc.tensor.matmul(acc[:, parity, :], h_sb[:, w, t, :],
                                            plain_t[:, slot(PLAIN, w, g), i, :],
                                            start=(w == 0 and t == 0), stop=(w == WINDOWS - 1 and t == TILES - 1))
                last.then_inc(pair_used, 1)

            def multiply_split(u, w, g, parity, first):
                k = SPLIT.index((w, g))
                if first:
                    pe.wait_ge(h_hi_ready, k + 1)
                pe.wait_ge(a_hi_ready, u * len(SPLIT) + k + 1)
                for i in range(2):
                    nc.tensor.matmul(acc[:, parity, :], h_hi[:, k, i, :], a_hi[:, k % RING, i, :],
                                     start=(w == 0 and g == 0 and i == 0), stop=False)
                if first:
                    pe.wait_ge(h_lo_ready, k + 1)
                for i in range(2):
                    nc.tensor.matmul(acc[:, parity, :], h_lo[:, k, i, :], a_hi[:, k % RING, i, :],
                                     start=False, stop=False)
                pe.wait_ge(a_lo_ready, u * len(SPLIT) + k + 1)
                for i in range(2):
                    last = nc.tensor.matmul(acc[:, parity, :], h_hi[:, k, i, :], a_lo[:, k % RING, i, :],
                                            start=False, stop=(w == WINDOWS - 1 and g == PAIRS - 1 and i == 1))
                last.then_inc(pair_used, 1)

            def turn_back(u, very_first):
                pe.wait_ge(acc_copied, u + 1)
                if not very_first:
                    pe.wait_ge(out_ready, u)
                columns = acc_sb[:, :].rearrange("f (p s) -> f s p", s=S)
                for s in range(S):
                    last = nc.tensor.transpose(back[:, s, :], columns[:, s, :], ident[:, :])
                last.then_inc(turned_back, 1)

            def chunk(u, parity, first=False, second=False):
                if not (first or second):
                    pe.wait_ge(acc_copied, u - 1)
                for w in range(WINDOWS):
                    for g in range(PAIRS):
                        multiply = multiply_split if (w, g) in SPLIT else multiply_plain
                        multiply(u, w, g, parity, first)
                    if w == COPY_AT and not first:
                        turn_back(u - 1, second)

            chunk(0, 0, first=True)
            pe.wait_ge(ident_ready, 1)
            chunk(1, 1, second=True)
            with pe.Fori(1, CHUNKS // 2) as two:
                chunk(2 * two, 0)
                chunk(2 * two + 1, 1)
            turn_back(CHUNKS - 1, False)


_INS = ['x', 'adj', 'L0_gnn_h']
_OUTS = [((8192, 128), 'float32')]


def kernel(**inputs):
    import numpy as _np
    import concourse.bacc as _bacc
    from concourse import mybir as _mybir
    from concourse.bass_utils import run_bass_kernel_spmd as _run

    nc = _bacc.Bacc("TRN2", target_bir_lowering=False, num_devices=1)
    arrays, args = {}, []
    for name in _INS:
        a = _np.ascontiguousarray(inputs[name])
        arrays[f"in_{name}_dram"] = a
        args.append(nc.dram_tensor(f"in_{name}_dram", a.shape, _mybir.dt.from_np(a.dtype), kind="ExternalInput").ap())
    for i, (shape, dtype) in enumerate(_OUTS):
        dt = _mybir.dt.from_np(_np.dtype(dtype))
        args.append(nc.dram_tensor(f"out_{i}_dram", shape, dt, kind="ExternalOutput").ap())
    gnn_layer_kernel(nc, *args)
    r = _run(nc, [arrays], core_ids=[0])
    got = tuple(r.results[0][f"out_{i}_dram"] for i in range(len(_OUTS)))
    return got[0]
```

```python
import concourse.bass as bass
from concourse import mybir
from contextlib import ExitStack


def gnn_layer_kernel(nc: bass.Bass, x: bass.AP, adj: bass.AP, L0_gnn_h: bass.AP, out: bass.AP):
    fp32 = mybir.dt.float32
    fp32r = mybir.dt.float32r
    ALU = mybir.AluOpType
    ACT = mybir.ActivationFunctionType

    ALPHA, EPS = 0.1, 1e-5
    P, QUAD = 128, 32
    N, F = x.shape
    NQ = P // QUAD
    KQ = N // NQ
    CHUNK = 512
    CHUNKS = N // CHUNK
    BLOCKS = CHUNK // QUAD
    W = 256
    WINDOWS = KQ // W
    TILES = W // QUAD
    PAIRS = TILES // 2
    CPAIRS = WINDOWS * PAIRS
    ADJ_RING = 4
    AHEAD = ADJ_RING - 1
    X_RING = 4
    RING = 4
    RAW_RING = 4
    PLAIN_RING = 4
    PIECES = 2
    PW = W // PIECES
    S = CHUNK // P
    LOADED = 16 * NQ

    COPY_AT = 2
    WRITE_AT = 5
    STORE_AT = 6
    FIRST_COPY_AT = 0
    FIRST_WRITE_AT = 2
    FIRST_STORE_AT = 3

    def is_split(w, g):
        return g >= 2 if w == 0 else g % 2 == 0 or (g == 1 and w in (2, 3, 5, 6))

    def on_vector(w, g):
        return g == 1 and w in (2, 5)

    class Turn:

        def __init__(self, chunks, windows):
            self.chunks, self.windows = chunks, windows
            pairs = [(v, g) for v in range(WINDOWS) for g in range(PAIRS)]
            self.split = [(v, g) for v, g in pairs if is_split(windows[v], g)]
            self.plain = [(v, g) for v, g in pairs if not is_split(windows[v], g)]
            self.on_vector = [(v, g) for v, g in pairs if on_vector(windows[v], g)]
            self.on_gpsimd = [(v, g) for v, g in self.split if (v, g) not in self.on_vector]

    HALF = WINDOWS // 2
    OPENING = [Turn([v % 2 for v in range(WINDOWS)], [b * HALF + v // 2 for v in range(WINDOWS)])
               for b in range(2)]
    REGULAR = Turn(None, list(range(WINDOWS)))
    SPLITS, PLAINS = len(REGULAR.split), len(REGULAR.plain)
    VECTORS, GPSIMDS = len(REGULAR.on_vector), len(REGULAR.on_gpsimd)
    assert SPLITS % RING == 0 and SPLITS % RAW_RING == 0 and PLAINS % PLAIN_RING == 0
    for turn in OPENING:
        assert len(turn.split) == SPLITS and len(turn.on_vector) == VECTORS
    assert not is_split(0, 0) and not is_split(WINDOWS - 1, PAIRS - 1)
    assert not any(on_vector(w, PAIRS - 1) for w in range(WINDOWS))

    def turn_of(b):
        if isinstance(b, int) and b < 3:
            return (OPENING + [REGULAR])[b], (OPENING[:1] + OPENING)[b]
        return REGULAR, REGULAR

    def place(b, v):
        turn, _ = turn_of(b)
        return (turn.chunks[v] if turn.chunks else b), turn.windows[v]

    H_SPLIT, H_PLAIN = REGULAR.split, REGULAR.plain

    MOMENTS_BEFORE = (2, 0)
    ROOT_AT = (1, 0)
    SCALES_AFTER = (3, 1)

    def next_layernorm(b, v):
        if isinstance(b, int) and b < 2 and v % 2 == 0 and turn_of(b)[0].windows[v] + 1 < WINDOWS:
            return turn_of(b)[0].windows[v] + 1
        return None

    def pair(b, v, g):
        return b * CPAIRS + v * PAIRS + g

    def held_slot_before(split, b, v, g):
        turn, before = turn_of(b)
        pairs, earlier = (turn.split, before.split) if split else (turn.plain, before.plain)
        i = pairs.index((v, g)) - (RING if split else PLAIN_RING)
        if i >= 0:
            return pair(b, *pairs[i])
        return None if isinstance(b, int) and b == 0 else pair(b - 1, *earlier[i])

    adj_v = adj.rearrange("(u j r) (q w c) -> u q w r j c", j=BLOCKS, r=QUAD, q=NQ, w=WINDOWS)
    x_k = x.rearrange("(q w t c) f -> q w c t f", q=NQ, w=WINDOWS, c=QUAD)
    x_m = x.rearrange("(u p s) f -> u p s f", p=P, s=S)
    h_m = L0_gnn_h.rearrange("(u p s) f -> u p s f", p=P, s=S)
    out_m = out.rearrange("(u p s) f -> u p s f", p=P, s=S)

    ctx = ExitStack()
    with ctx:
        def sb(name, shape, dt=fp32):
            return ctx.enter_context(nc.sbuf_tensor(name, shape, dt))

        def sem(name):
            return ctx.enter_context(nc.semaphore(name))

        adj_sb = sb("adj_sb", [P, ADJ_RING, BLOCKS, W])
        plain_t = sb("plain_t", [P, PLAIN_RING, 2, CHUNK])
        raw_t = sb("raw_t", [P, RAW_RING, 2, CHUNK])
        a_hi = sb("a_hi", [P, RING, 2, CHUNK], fp32r)
        a_lo = sb("a_lo", [P, RING, 2, CHUNK], fp32r)
        x_sb = sb("x_sb", [P, X_RING, TILES, F])
        h_plain = sb("h_plain", [P, PLAINS, 2, F])
        h_hi = sb("h_hi", [P, SPLITS, 2, F], fp32r)
        h_lo = sb("h_lo", [P, SPLITS, 2, F], fp32r)
        acc_sb = sb("acc_sb", [P, CHUNK])
        x_res = sb("x_res", [P, S, F])
        h_res = sb("h_res", [P, S, F])
        out_sb = sb("out_sb", [P, S, F])
        ident = sb("ident", [P, P])
        stats = sb("stats", [P, TILES, 6])
        moments = sb("moments", [P, WINDOWS, TILES, 2])
        var_eps = sb("var_eps", [P, WINDOWS, TILES])
        root = sb("root", [P, WINDOWS, TILES])
        recip = sb("recip", [P, TILES])
        newton = sb("newton", [P, TILES])
        rstd = sb("rstd", [P, WINDOWS, TILES])
        shift = sb("shift", [P, WINDOWS, TILES])

        acc = ctx.enter_context(nc.psum_tensor("acc", [P, 2, CHUNK], fp32))
        back = ctx.enter_context(nc.psum_tensor("back", [P, S, F], fp32))

        first_piece_loaded = [sem(f"first_piece_loaded{b}") for b in range(PIECES)]
        last_piece_loaded = [sem(f"last_piece_loaded{b}") for b in range(PIECES)]
        window_loaded = [sem(f"window_loaded{w}") for w in range(ADJ_RING)]
        x_loaded = [sem(f"x_loaded{w}") for w in range(WINDOWS)]
        ident_zeroed = sem("ident_zeroed")
        ident_ready = sem("ident_ready")
        stat_step = sem("stat_step")
        var_ready = sem("var_ready")
        root_ready = sem("root_ready")
        scales_ready = sem("scales_ready")
        h_ready = sem("h_ready")
        h_hi_ready = sem("h_hi_ready")
        h_lo_ready = sem("h_lo_ready")
        pair_transposed = sem("pair_transposed")
        a_hi_ready = sem("a_hi_ready")
        a_lo_gpsimd = sem("a_lo_gpsimd")
        a_lo_vector = sem("a_lo_vector")
        pair_used = sem("pair_used")
        acc_copied = sem("acc_copied")
        turned_back = sem("turned_back")
        res_loaded = sem("res_loaded")
        res_summed = sem("res_summed")
        out_ready = sem("out_ready")
        out_stored = sem("out_stored")

        block = ctx.enter_context(nc.Block())

        def load_window(eng, quadrants, b, v):
            u, w = place(b, v)
            for q in quadrants:
                eng.dma_start(adj_sb[q * QUAD:(q + 1) * QUAD, v % ADJ_RING, :, :],
                              adj_v[u, q, w]).then_inc(window_loaded[v % ADJ_RING], 16)

        def load_in_pieces(eng, quadrants, b, v, loaded):
            u, w = place(b, v)
            for k in range(PIECES):
                for q in quadrants:
                    eng.dma_start(adj_sb[q * QUAD:(q + 1) * QUAD, v % ADJ_RING, :, k * PW:(k + 1) * PW],
                                  adj_v[u, q, w, :, :, k * PW:(k + 1) * PW]).then_inc(loaded[k], 16)

        def wait_for_low_part(eng, b, v, g):
            turn, _ = turn_of(b)
            if (v, g) in turn.on_vector:
                eng.wait_ge(a_lo_vector, b * VECTORS + turn.on_vector.index((v, g)) + 1)
            else:
                eng.wait_ge(a_lo_gpsimd, b * GPSIMDS + turn.on_gpsimd.index((v, g)) + 1)

        @block.gpsimd
        def _(pool):
            nc.gpsimd.memset(ident[:, :], 0.0).then_inc(ident_zeroed, 1)
            pool.wait_ge(ident_zeroed, 1)
            nc.gpsimd.affine_select(out=ident[:, :], in_=ident[:, :], compare_op=ALU.not_equal, fill=1.0,
                                    base=0, pattern=[[-1, P]], channel_multiplier=1).then_inc(ident_ready, 1)

            def low_part(b, v, g):
                i = turn_of(b)[0].split.index((v, g))
                pool.wait_ge(a_hi_ready, b * SPLITS + i + 1)
                nc.gpsimd.tensor_tensor(a_lo[:, i % RING, :, :], raw_t[:, i % RAW_RING, :, :],
                                        a_hi[:, i % RING, :, :].bitcast(fp32), ALU.subtract).then_inc(a_lo_gpsimd, 1)

            def low_part_of_h(k):
                w, g = H_SPLIT[k]
                pool.wait_ge(h_hi_ready, k + 1)
                nc.gpsimd.tensor_tensor(h_lo[:, k, :, :], x_sb[:, w % X_RING, 2 * g:2 * g + 2, :],
                                        h_hi[:, k, :, :].bitcast(fp32), ALU.subtract).then_inc(h_lo_ready, 1)

            for b in range(2):
                for v, g in OPENING[b].split:
                    if v % 2 == 0:
                        low_part_of_h(H_SPLIT.index((OPENING[b].windows[v], g)))
                    if (v, g) in OPENING[b].on_gpsimd:
                        low_part(b, v, g)
            with pool.Fori(2, CHUNKS) as b:
                for v, g in REGULAR.on_gpsimd:
                    low_part(b, v, g)

        @block.sync
        def _(sp):
            def load_x_window(w):
                for q in (0, 2, 1, 3):
                    sp.dma_start(x_sb[q * QUAD:(q + 1) * QUAD, w % X_RING, :, :], x_k[q, w]).then_inc(x_loaded[w], 16)

            load_x_window(0)
            load_in_pieces(sp, (0, 1), 0, 0, first_piece_loaded)
            for b in range(2):
                for v in range(WINDOWS):
                    w = next_layernorm(b, v)
                    if w is not None:
                        if w >= X_RING:
                            sp.wait_ge(h_ready, (w - X_RING + 1) * TILES)
                            sp.wait_ge(h_lo_ready, sum(of <= w - X_RING for of, _ in H_SPLIT))
                        load_x_window(w)
                    if b or v:
                        if b or v >= ADJ_RING:
                            sp.wait_ge(pair_transposed, pair(b, v - ADJ_RING + 1, 0))
                        load_window(sp, (0, 1), b, v)
            with sp.Fori(2, CHUNKS - 1) as b:
                for v in range(WINDOWS):
                    sp.wait_ge(pair_transposed, pair(b, v - ADJ_RING + 1, 0))
                    load_window(sp, (0, 1), b, v)
            for v in range(WINDOWS):
                sp.wait_ge(pair_transposed, pair(CHUNKS - 1, v - ADJ_RING + 1, 0))
                if v < WINDOWS - 1:
                    load_window(sp, (0, 1), CHUNKS - 1, v)
                else:
                    load_in_pieces(sp, (0, 1), CHUNKS - 1, v, last_piece_loaded)

        @block.scalar
        def _(act):
            load_in_pieces(act, (2, 3), 0, 0, first_piece_loaded)
            load_window(act, (2, 3), 0, 1)

            def load_ahead(b, v, last):
                if isinstance(b, int) and b == 0 and v == 0:
                    for ahead in range(2, AHEAD + 1):
                        load_window(act, (2, 3), 0, ahead)
                elif v + AHEAD < WINDOWS:
                    act.wait_ge(pair_transposed, pair(b, v, 0))
                    if last and v + AHEAD == WINDOWS - 1:
                        load_in_pieces(act, (2, 3), b, v + AHEAD, last_piece_loaded)
                    else:
                        load_window(act, (2, 3), b, v + AHEAD)
                elif not last:
                    act.wait_ge(pair_transposed, pair(b, v, 0))
                    load_window(act, (2, 3), b + 1, v + AHEAD - WINDOWS)

            def take_root(w):
                act.wait_ge(var_ready, w + 1)
                nc.scalar.activation(root[:, w, :], var_eps[:, w, :], ACT.Sqrt).then_inc(root_ready, 1)

            def make_h(w, g):
                act.wait_ge(scales_ready, w + 1)
                for i in range(2):
                    t = 2 * g + i
                    x_tile = x_sb[:, w % X_RING, t, :]
                    to = x_tile if is_split(w, g) else h_plain[:, H_PLAIN.index((w, g)), i, :]
                    nc.scalar.activation(to, x_tile, ACT.Relu, bias=shift[:, w, t:t + 1],
                                         scale=rstd[:, w, t:t + 1]).then_inc(h_ready, 1)
                if is_split(w, g):
                    act.wait_ge(h_ready, w * TILES + 2 * g + 2)
                    nc.scalar.copy(h_hi[:, H_SPLIT.index((w, g)), :, :],
                                   x_sb[:, w % X_RING, 2 * g:2 * g + 2, :]).then_inc(h_hi_ready, 1)

            def high_part(b, v, g):
                i = turn_of(b)[0].split.index((v, g))
                act.wait_ge(pair_transposed, pair(b, v, g) + 1)
                held = held_slot_before(True, b, v, g)
                if held is not None:
                    act.wait_ge(pair_used, held + 1)
                nc.scalar.copy(a_hi[:, i % RING, :, :], raw_t[:, i % RAW_RING, :, :]).then_inc(a_hi_ready, 1)

            def load_residual(u, very_first):
                if not very_first:
                    act.wait_ge(out_ready, u)
                    act.wait_ge(out_stored, 16 * u)
                act.dma_start(x_res[:, :, :], x_m[u]).then_inc(res_loaded, 16)
                act.dma_start(h_res[:, :, :], h_m[u]).then_inc(res_loaded, 16)

            def copy_acc(u, parity, very_first):
                act.wait_ge(pair_used, pair(1, WINDOWS - 1, 0) if very_first else pair(u + 1, 0, 0))
                if not very_first:
                    act.wait_ge(turned_back, u)
                nc.scalar.copy(acc_sb[:, :], acc[:, parity, :]).then_inc(acc_copied, 1)

            def store(u):
                act.wait_ge(out_ready, u + 1)
                act.dma_start(out_m[u], out_sb[:, :, :]).then_inc(out_stored, 16)

            def split_turn(b, parity, last=False):
                opening = isinstance(b, int) and b < 2
                for v in range(WINDOWS):
                    load_ahead(b, v, last)
                    if isinstance(b, int) and b == 1 and v == 0:
                        load_residual(0, True)
                    elif not opening and v == 0 and not (isinstance(b, int) and b == 2):
                        load_residual(b - 1, False)
                    for g in range(PAIRS):
                        if opening and v % 2 == 0:
                            make_h(place(b, v)[1], g)
                        if is_split(place(b, v)[1], g):
                            high_part(b, v, g)
                        if next_layernorm(b, v) is not None and g == ROOT_AT[b > 0 or v > 0]:
                            take_root(next_layernorm(b, v))
                    if isinstance(b, int) and b == 2 and v == FIRST_COPY_AT:
                        copy_acc(0, 0, True)
                    if not opening and v == COPY_AT:
                        copy_acc(b - 1, 1 - parity, False)
                    if isinstance(b, int) and b == 2 and v == FIRST_STORE_AT:
                        store(0)
                        load_residual(1, False)
                    elif not opening and v == STORE_AT:
                        store(b - 1)
                        if last:
                            load_residual(b, False)

            take_root(0)
            for b in range(4):
                split_turn(b, b % 2)
            with act.Fori(2, CHUNKS // 2 - 1) as two:
                split_turn(2 * two, 0)
                split_turn(2 * two + 1, 1)
            split_turn(CHUNKS - 2, 0)
            split_turn(CHUNKS - 1, 1, last=True)
            copy_acc(CHUNKS - 1, 1, False)
            store(CHUNKS - 1)
            act.wait_ge(out_stored, 16 * CHUNKS)

        @block.vector
        def _(dve):
            steps = [0]

            def step(ins):
                steps[0] += 1
                ins.then_inc(stat_step, 1)
                dve.wait_ge(stat_step, steps[0])

            def layernorm_moments(w):
                dve.wait_ge(x_loaded[w], LOADED)
                for t in range(TILES):
                    last = nc.vector.bn_stats(stats[:, t, :], x_sb[:, w % X_RING, t, :])
                step(last)
                for t in range(TILES):
                    last = nc.vector.bn_aggr(moments[:, w, t, :], stats[:, t, :])
                step(last)
                nc.vector.tensor_scalar(var_eps[:, w, :], moments[:, w, :, 1], EPS, None,
                                        ALU.add).then_inc(var_ready, 1)

            def layernorm_scales(w):
                dve.wait_ge(root_ready, w + 1)
                step(nc.vector.reciprocal(recip[:, :], root[:, w, :]))
                step(nc.vector.tensor_tensor(newton[:, :], var_eps[:, w, :], recip[:, :], ALU.mult))
                step(nc.vector.tensor_tensor(newton[:, :], newton[:, :], root[:, w, :], ALU.add))
                step(nc.vector.tensor_scalar(newton[:, :], newton[:, :], 0.5, None, ALU.mult))
                step(nc.vector.reciprocal(rstd[:, w, :], newton[:, :]))
                nc.vector.scalar_tensor_tensor(out=shift[:, w, :], in0=moments[:, w, :, 0], scalar=-1.0,
                                               in1=rstd[:, w, :], op0=ALU.mult,
                                               op1=ALU.mult).then_inc(scales_ready, 1)

            def transpose_pair(b, v, g):
                turn, before = turn_of(b)
                if (v, g) in turn.split:
                    i = turn.split.index((v, g))
                    to = raw_t[:, i % RAW_RING, :, :]
                    if i >= RAW_RING:
                        wait_for_low_part(dve, b, *turn.split[i - RAW_RING])
                    elif not (isinstance(b, int) and b == 0):
                        wait_for_low_part(dve, b - 1, *before.split[i - RAW_RING])
                else:
                    i = turn.plain.index((v, g))
                    to = plain_t[:, i % PLAIN_RING, :, :]
                    held = held_slot_before(False, b, v, g)
                    if held is not None:
                        dve.wait_ge(pair_used, held + 1)
                blocks = adj_sb[:, v % ADJ_RING, :, 2 * g * QUAD:2 * (g + 1) * QUAD]
                nc.vector.transpose(to.rearrange("p t (j r) -> p t j r", r=QUAD),
                                    blocks.rearrange("p j (t c) -> p t j c", c=QUAD)).then_inc(pair_transposed, 1)

            def low_part(b, v, g):
                i = turn_of(b)[0].split.index((v, g))
                dve.wait_ge(a_hi_ready, b * SPLITS + i + 1)
                nc.vector.tensor_tensor(a_lo[:, i % RING, :, :], raw_t[:, i % RAW_RING, :, :],
                                        a_hi[:, i % RING, :, :].bitcast(fp32), ALU.subtract).then_inc(a_lo_vector, 1)

            def transpose_window(b, v, pieces=None):
                turn, _ = turn_of(b)
                if pieces is None:
                    loads = b * (WINDOWS // ADJ_RING) + v // ADJ_RING + (v % ADJ_RING > 0)
                    dve.wait_ge(window_loaded[v % ADJ_RING], loads * LOADED)
                for g in range(PAIRS):
                    if pieces is not None and g % (PAIRS // PIECES) == 0:
                        dve.wait_ge(pieces[g // (PAIRS // PIECES)], LOADED)
                    w = next_layernorm(b, v)
                    if w is not None and g == MOMENTS_BEFORE[b > 0 or v > 0]:
                        layernorm_moments(w)
                    transpose_pair(b, v, g)
                    if g > 0 and (v, g - 1) in turn.on_vector:
                        low_part(b, v, g - 1)
                    if w is not None and g == SCALES_AFTER[b > 0 or v > 0]:
                        layernorm_scales(w)

            def write_out(u):
                dve.wait_ge(res_loaded, 32 * (u + 1))
                nc.vector.scalar_tensor_tensor(out=x_res[:, :, :], in0=h_res[:, :, :], scalar=ALPHA,
                                               in1=x_res[:, :, :], op0=ALU.mult, op1=ALU.add).then_inc(res_summed, 1)
                dve.wait_ge(res_summed, u + 1)
                dve.wait_ge(turned_back, u + 1)
                nc.vector.scalar_tensor_tensor(out=out_sb[:, :, :], in0=back[:, :, :], scalar=1.0 - ALPHA,
                                               in1=x_res[:, :, :], op0=ALU.mult, op1=ALU.add).then_inc(out_ready, 1)

            layernorm_moments(0)
            layernorm_scales(0)
            for b in range(3):
                for v in range(WINDOWS):
                    transpose_window(b, v, None if b or v else first_piece_loaded)
                    if b == 2 and v == FIRST_WRITE_AT:
                        write_out(0)
                    if b == 2 and v == WRITE_AT:
                        write_out(1)
            with dve.Fori(3, CHUNKS - 1) as b:
                for v in range(WINDOWS):
                    transpose_window(b, v)
                    if v == WRITE_AT:
                        write_out(b - 1)
            for v in range(WINDOWS):
                transpose_window(CHUNKS - 1, v, last_piece_loaded if v == WINDOWS - 1 else None)
                if v == WRITE_AT:
                    write_out(CHUNKS - 2)
            write_out(CHUNKS - 1)

        @block.tensor
        def _(pe):
            def multiply_plain(b, v, g, parity):
                u, w = place(b, v)
                pe.wait_ge(pair_transposed, pair(b, v, g) + 1)
                i_slot = turn_of(b)[0].plain.index((v, g)) % PLAIN_RING
                for i in range(2):
                    t = 2 * g + i
                    if isinstance(b, int) and b < 2 and v % 2 == 0:
                        pe.wait_ge(h_ready, w * TILES + t + 1)
                    last = nc.tensor.matmul(acc[:, parity, :], h_plain[:, H_PLAIN.index((w, g)), i, :],
                                            plain_t[:, i_slot, i, :],
                                            start=(w == 0 and t == 0), stop=(w == WINDOWS - 1 and t == TILES - 1))
                last.then_inc(pair_used, 1)

            def multiply_split(b, v, g, parity):
                u, w = place(b, v)
                k = H_SPLIT.index((w, g))
                n = turn_of(b)[0].split.index((v, g))
                makes_h = isinstance(b, int) and b < 2 and v % 2 == 0
                if makes_h:
                    pe.wait_ge(h_hi_ready, k + 1)
                pe.wait_ge(a_hi_ready, b * SPLITS + n + 1)
                for i in range(2):
                    nc.tensor.matmul(acc[:, parity, :], h_hi[:, k, i, :], a_hi[:, n % RING, i, :],
                                     start=False, stop=False)
                if makes_h:
                    pe.wait_ge(h_lo_ready, k + 1)
                for i in range(2):
                    nc.tensor.matmul(acc[:, parity, :], h_lo[:, k, i, :], a_hi[:, n % RING, i, :],
                                     start=False, stop=False)
                wait_for_low_part(pe, b, v, g)
                for i in range(2):
                    last = nc.tensor.matmul(acc[:, parity, :], h_hi[:, k, i, :], a_lo[:, n % RING, i, :],
                                            start=False, stop=False)
                last.then_inc(pair_used, 1)

            def turn_back(u, very_first):
                pe.wait_ge(acc_copied, u + 1)
                if not very_first:
                    pe.wait_ge(out_ready, u)
                columns = acc_sb[:, :].rearrange("f (p s) -> f s p", s=S)
                for s in range(S):
                    last = nc.tensor.transpose(back[:, s, :], columns[:, s, :], ident[:, :])
                last.then_inc(turned_back, 1)

            def multiply_turn(b, parity):
                opening = isinstance(b, int) and b < 2
                if not opening:
                    pe.wait_ge(acc_copied, b - 1)
                for v in range(WINDOWS):
                    for g in range(PAIRS):
                        multiply = multiply_split if is_split(place(b, v)[1], g) else multiply_plain
                        multiply(b, v, g, v % 2 if opening else parity)
                    if v == COPY_AT and not opening:
                        turn_back(b - 1, False)

            multiply_turn(0, None)
            multiply_turn(1, None)
            pe.wait_ge(ident_ready, 1)
            turn_back(0, True)
            with pe.Fori(1, CHUNKS // 2) as two:
                multiply_turn(2 * two, 0)
                multiply_turn(2 * two + 1, 1)
            turn_back(CHUNKS - 1, False)


_INS = ['x', 'adj', 'L0_gnn_h']
_OUTS = [((8192, 128), 'float32')]


def kernel(**inputs):
    import numpy as _np
    import concourse.bacc as _bacc
    from concourse import mybir as _mybir
    from concourse.bass_utils import run_bass_kernel_spmd as _run

    nc = _bacc.Bacc("TRN2", target_bir_lowering=False, num_devices=1)
    arrays, args = {}, []
    for name in _INS:
        a = _np.ascontiguousarray(inputs[name])
        arrays[f"in_{name}_dram"] = a
        args.append(nc.dram_tensor(f"in_{name}_dram", a.shape, _mybir.dt.from_np(a.dtype), kind="ExternalInput").ap())
    for i, (shape, dtype) in enumerate(_OUTS):
        dt = _mybir.dt.from_np(_np.dtype(dtype))
        args.append(nc.dram_tensor(f"out_{i}_dram", shape, dt, kind="ExternalOutput").ap())
    gnn_layer_kernel(nc, *args)
    r = _run(nc, [arrays], core_ids=[0])
    got = tuple(r.results[0][f"out_{i}_dram"] for i in range(len(_OUTS)))
    return got[0]
```
